# Optimizing a Trainium2 kernel written in Bass

```python
import numpy as np
import jax
import jax.numpy as jnp

def _softmax(x, axis=-1):
    return jax.nn.softmax(x, axis=axis)

def _gelu(x):
    return jax.nn.gelu(x, approximate=True)

def _silu(x):
    return jax.nn.silu(x)

def _sigmoid(x):
    return jax.nn.sigmoid(x)

def _layernorm(x, axis=-1, eps=1e-05):
    m = jnp.mean(x, axis=axis, keepdims=True)
    v = jnp.var(x, axis=axis, keepdims=True)
    return (x - m) / jnp.sqrt(v + eps)

def _scatter_add(tgt, idx, src, axis=0):
    return tgt.at[idx].add(src)

def _segment_sum(src, seg, n):
    return jax.ops.segment_sum(src, seg, n)
kernel_name = 'mk_cond_seq_d1_seqx_r2_a484a7'

def setup_inputs(seed: int=0):
    np.random.seed(seed)
    _w = jnp.asarray

    def _rec_inputs():
        import jax
        import jax.numpy as jnp
        _rk = jax.random.key(seed)
        x = -7.109e-05 + 0.9999 * jax.random.normal(jax.random.fold_in(_rk, 1), (16, 512, 512), jnp.float32)
        _lenS = 512 - jax.random.randint(jax.random.fold_in(_rk, 7), (16,), 0, max(1, 512 // 4) + 1, jnp.int32)
        _lenS2 = 512 - jax.random.randint(jax.random.fold_in(_rk, 8), (16,), 0, max(1, 512 // 4) + 1, jnp.int32)
        itok_B_0_2 = jax.random.randint(jax.random.fold_in(_rk, 11), (16,), 0, 3, jnp.int32)
        return (x, itok_B_0_2)
    x, itok_B_0_2 = _rec_inputs()

    def _L0_cond_setup():
        import jax, jax.numpy as jnp
        import numpy as np
        H = 512
        EPS = 1e-05

        def _gelu(x):
            return jax.nn.gelu(x, approximate=False)
        key = jax.random.key(seed)
        ks = jax.random.split(key, 16)
        s = 1.0 / np.sqrt(H)
        inp = {'x': jax.random.normal(ks[0], (64, 512, H), dtype=jnp.float32), 'condition': jax.random.randint(ks[1], (64,), 0, 3), 'w1_nr': jax.random.normal(ks[2], (H, H), dtype=jnp.float32) * s, 'b1_nr': jnp.zeros((H,), dtype=jnp.float32), 'w2_nr': jax.random.normal(ks[3], (H, H), dtype=jnp.float32) * s, 'b2_nr': jnp.zeros((H,), dtype=jnp.float32), 'w1_tsr': jax.random.normal(ks[4], (H, H), dtype=jnp.float32) * s, 'b1_tsr': jnp.zeros((H,), dtype=jnp.float32), 'w2_tsr': jax.random.normal(ks[5], (H, H), dtype=jnp.float32) * s, 'b2_tsr': jnp.zeros((H,), dtype=jnp.float32), 'w1_sr': jax.random.normal(ks[6], (H, 2 * H), dtype=jnp.float32) * s, 'b1_sr': jnp.zeros((2 * H,), dtype=jnp.float32), 'w2_sr': jax.random.normal(ks[7], (2 * H, H), dtype=jnp.float32) * (1.0 / np.sqrt(2 * H)), 'b2_sr': jnp.zeros((H,), dtype=jnp.float32), 'w3_sr': jax.random.normal(ks[8], (H, H), dtype=jnp.float32) * s, 'b3_sr': jnp.zeros((H,), dtype=jnp.float32), 'gamma': jnp.ones((H,), dtype=jnp.float32), 'beta': jnp.zeros((H,), dtype=jnp.float32)}
        return inp
    _L0_cond_all = _L0_cond_setup()
    _L0_cond_in = {k: v for k, v in _L0_cond_all.items() if k in ('w1_nr', 'b1_nr', 'w2_nr', 'b2_nr', 'w1_tsr', 'b1_tsr', 'w2_tsr', 'b2_tsr', 'w1_sr', 'b1_sr', 'w2_sr', 'b2_sr', 'w3_sr', 'b3_sr', 'gamma', 'beta')}
    del _L0_cond_all
    return {'x': x, 'itok_B_0_2': itok_B_0_2, 'L0_cond_w1_nr': _L0_cond_in['w1_nr'], 'L0_cond_b1_nr': _L0_cond_in['b1_nr'], 'L0_cond_w2_nr': _L0_cond_in['w2_nr'], 'L0_cond_b2_nr': _L0_cond_in['b2_nr'], 'L0_cond_w1_tsr': _L0_cond_in['w1_tsr'], 'L0_cond_b1_tsr': _L0_cond_in['b1_tsr'], 'L0_cond_w2_tsr': _L0_cond_in['w2_tsr'], 'L0_cond_b2_tsr': _L0_cond_in['b2_tsr'], 'L0_cond_w1_sr': _L0_cond_in['w1_sr'], 'L0_cond_b1_sr': _L0_cond_in['b1_sr'], 'L0_cond_w2_sr': _L0_cond_in['w2_sr'], 'L0_cond_b2_sr': _L0_cond_in['b2_sr'], 'L0_cond_w3_sr': _L0_cond_in['w3_sr'], 'L0_cond_b3_sr': _L0_cond_in['b3_sr'], 'L0_cond_gamma': _L0_cond_in['gamma'], 'L0_cond_beta': _L0_cond_in['beta']}

def reference(x, itok_B_0_2, L0_cond_w1_nr, L0_cond_b1_nr, L0_cond_w2_nr, L0_cond_b2_nr, L0_cond_w1_tsr, L0_cond_b1_tsr, L0_cond_w2_tsr, L0_cond_b2_tsr, L0_cond_w1_sr, L0_cond_b1_sr, L0_cond_w2_sr, L0_cond_b2_sr, L0_cond_w3_sr, L0_cond_b3_sr, L0_cond_gamma, L0_cond_beta):
    import jax
    import jax.numpy as jnp

    def _L0_cond_ref(x, condition, w1_nr, b1_nr, w2_nr, b2_nr, w1_tsr, b1_tsr, w2_tsr, b2_tsr, w1_sr, b1_sr, w2_sr, b2_sr, w3_sr, b3_sr, gamma, beta):
        import jax, jax.numpy as jnp
        import numpy as np
        H = 512
        EPS = 1e-05

        def _gelu(x):
            return jax.nn.gelu(x, approximate=False)
        out_nr = _gelu(jnp.einsum('bth,hk->btk', x, w1_nr) + b1_nr)
        out_nr = jnp.einsum('bth,hk->btk', out_nr, w2_nr) + b2_nr
        out_tsr = _gelu(jnp.einsum('bth,hk->btk', x, w1_tsr) + b1_tsr)
        out_tsr = jnp.einsum('bth,hk->btk', out_tsr, w2_tsr) + b2_tsr
        h = _gelu(jnp.einsum('bth,hk->btk', x, w1_sr) + b1_sr)
        h = _gelu(jnp.einsum('bth,hk->btk', h, w2_sr) + b2_sr)
        out_sr = jnp.einsum('bth,hk->btk', h, w3_sr) + b3_sr
        c = condition[:, None, None]
        out = jnp.where(c == 0, out_nr, jnp.where(c == 1, out_tsr, jnp.where(c == 2, out_sr, jnp.zeros_like(x))))
        y = x + out
        mu = jnp.mean(y, axis=-1, keepdims=True)
        var = jnp.mean((y - mu) ** 2, axis=-1, keepdims=True)
        return (y - mu) * jax.lax.rsqrt(var + EPS) * gamma + beta
    x = _L0_cond_ref(x, itok_B_0_2, L0_cond_w1_nr, L0_cond_b1_nr, L0_cond_w2_nr, L0_cond_b2_nr, L0_cond_w1_tsr, L0_cond_b1_tsr, L0_cond_w2_tsr, L0_cond_b2_tsr, L0_cond_w1_sr, L0_cond_b1_sr, L0_cond_w2_sr, L0_cond_b2_sr, L0_cond_w3_sr, L0_cond_b3_sr, L0_cond_gamma, L0_cond_beta)
    return x

_drawn_inputs = setup_inputs


def setup_inputs(seed=0):
    import zlib

    import numpy as np

    out = dict(_drawn_inputs(seed))
    spreads = {'L0_cond_b1_nr': (0.0, 0.1),
     'L0_cond_b2_nr': (0.0, 0.1),
     'L0_cond_b1_tsr': (0.0, 0.332),
     'L0_cond_b2_tsr': (0.0, 0.1),
     'L0_cond_b1_sr': (0.0, 0.319),
     'L0_cond_b2_sr': (0.0, 0.1),
     'L0_cond_b3_sr': (0.0, 0.1),
     'L0_cond_gamma': (1.0, 0.2),
     'L0_cond_beta': (0.0, 0.1)}
    factors = {}
    for name, (base, spread) in spreads.items():
        noise = np.random.default_rng([zlib.crc32(name.encode()), seed]).standard_normal(out[name].shape)
        drawn = base * np.exp(spread * noise) if base else spread * noise
        out[name] = jnp.asarray(drawn.astype(out[name].dtype))
    for name, factor in factors.items():
        out[name] = (out[name] * factor).astype(out[name].dtype)
    return out
```

```python
from contextlib import ExitStack

import concourse.bass as bass
from concourse import mybir

P = 128
NBATCH = 16
T = 512
H = 512
HC = H // P
TT = T // P
EPS = 1e-5
NR, TSR, SR, NONE = 0, 1, 2, 3

W1, W2, W3 = {NR: 0, TSR: 8, SR: 16}, {NR: 4, TSR: 12, SR: 24}, {SR: 32}
N_WCHUNK = 36
B1, B2 = {NR: 0, TSR: 4, SR: 8}, {SR: 16}
N_BCOL = 20
R_GAMMA, R_BETA, N_ROW = 3, 4, 5


def conditional_mlp(nc, x, x_t, cond, weights, bias_cols, rows, out):
    fp32, fp32r, i32 = mybir.dt.float32, mybir.dt.float32r, mybir.dt.int32
    ALU, ACT = mybir.AluOpType, mybir.ActivationFunctionType
    ctx = ExitStack()
    with ctx:
        def sb(name, shape, dt=fp32):
            return ctx.enter_context(nc.sbuf_tensor(name, shape, dt))

        def sem(name):
            return ctx.enter_context(nc.semaphore(name))

        w_hi = sb("w_hi", [P, N_WCHUNK, H], fp32r)
        w_lo = sb("w_lo", [P, N_WCHUNK, H], fp32r)
        stage = sb("stage", [P, 2, 2, T])
        x_hi = sb("x_hi", [P, HC, T], fp32r)
        x_lo = sb("x_lo", [P, HC, T], fp32r)
        g_hi = sb("g_hi", [P, 4, T], fp32r)
        g_lo = sb("g_lo", [P, 4, T], fp32r)
        y = sb("y", [P, TT, H])
        row = sb("row", [P, N_ROW, H])
        bcol = sb("bcol", [P, N_BCOL])
        cond_sb = sb("cond_sb", [1, NBATCH], i32)
        bn = sb("bn", [P, TT, 6])
        mv = sb("mv", [P, TT, 2])
        var_eps = sb("var_eps", [P, TT])
        rstd = sb("rstd", [P, TT])
        power = sb("power", [P, TT])
        bank = [ctx.enter_context(nc.psum_tensor(f"bank{i}", [P, 512], fp32)) for i in range(8)]

        g_hi32 = g_hi[:, :, :].bitcast(fp32)
        x_hi32 = x_hi[:, :, :].bitcast(fp32)
        w_hi32 = w_hi[:, :, :].bitcast(fp32)

        s_const = sem("s_const")
        s_power = sem("s_power")
        s_full = [sem("s_full0"), sem("s_full1")]
        s_hi = sem("s_hi")
        s_wsplit = sem("s_wsplit")
        s_xs = sem("s_xs")
        s_stage = sem("s_stage")
        s_h = sem("s_h")
        s_g = sem("s_g")
        s_gs = sem("s_gs")
        s_y = sem("s_y")
        s_acc = sem("s_acc")
        s_row = [sem("s_row0"), sem("s_row1")]
        s_xb = sem("s_xb")
        s_ev = sem("s_ev")
        s_bn = sem("s_bn")
        s_mv = sem("s_mv")
        s_var = sem("s_var")
        s_eps = sem("s_eps")
        s_rstd = sem("s_rstd")
        s_v = sem("s_v")
        s_n = sem("s_n")
        s_fin = sem("s_fin")
        s_out = [sem("s_out0"), sem("s_out1")]

        def take(eng, s, n=1):
            eng.wait_ge(s, n)
            eng.sem_inc(s, -n)

        def dispatch(eng, b, body):
            c = eng.value_load(cond_sb[0:1, bass.ds(b, 1)])
            with eng.If(c == NR):
                body(NR)
            with eng.Else():
                with eng.If(c == TSR):
                    body(TSR)
                with eng.Else():
                    with eng.If(c == SR):
                        body(SR)
                    with eng.Else():
                        body(NONE)

        def over_batches(eng, step):
            with eng.Fori(0, NBATCH - 1) as b:
                step(b, False)
            step(NBATCH - 1, True)

        def hidden_bank(kind, j):
            if kind != SR:
                return j
            return (3, 2)[j] if j < 2 else 4 + (j - 2) % 4

        block = ctx.enter_context(nc.Block())

        @block.sync
        def _(eng):
            x_rows = x.rearrange("b (p c) h -> b p c h", c=TT)
            out_rows = out.rearrange("b (p c) h -> b p c h", c=TT)
            x_halves = x_t.rearrange("b f p n -> (b f) p n")

            def load_stage(n, src):
                eng.dma_start(stage[:, n % 2, :, :].rearrange("p c t -> p (c t)"), src).then_inc(s_full[n % 2], 16)

            def load_rows(b, f):
                eng.dma_start(y[:, 2 * f:2 * f + 2, :], x_rows[b, :, 2 * f:2 * f + 2, :]).then_inc(s_row[f], 16)

            for f in range(2):
                load_stage(f, x_halves[f])
            eng.dma_start(cond_sb[:, :], cond.rearrange("(a b) -> a b", a=1)).then_inc(s_const, 16)
            eng.dma_start(bcol[:, :], bias_cols).then_inc(s_const, 16)
            for u in range(N_WCHUNK // 2):
                eng.wait_ge(s_wsplit, u + 1)
                load_stage(u, weights[u])
                if u == 0:
                    eng.dma_start(row[:, :, :], rows.rearrange("(a r) h -> a r h", a=1).to_broadcast([P, N_ROW, H])).then_inc(s_const, 16)
                    for f in range(2):
                        load_rows(0, f)
            eng.wait_ge(s_wsplit, 2 + N_WCHUNK // 2)

            def step(b, last):
                if not last:
                    for f in range(2):
                        take(eng, s_stage)
                        load_stage(f, x_halves[bass.ds(b * 2 + (2 + f), 1), :, :].rearrange("a p n -> p (a n)"))
                for f in range(2):
                    take(eng, s_fin, 2)
                    eng.dma_start(out_rows[bass.ds(b, 1), :, 2 * f:2 * f + 2, :].rearrange("a p c h -> p (a c) h"), y[:, 2 * f:2 * f + 2, :]).then_inc(s_out[f], 16)
                for f in range(2):
                    take(eng, s_out[f], 16)
                    if not last:
                        eng.dma_start(y[:, 2 * f:2 * f + 2, :], x_rows[bass.ds(b + 1, 1), :, 2 * f:2 * f + 2, :].rearrange("a p c h -> p (a c) h")).then_inc(s_row[f], 16)

            over_batches(eng, step)

        @block.tensor
        def _(eng):
            def product(dst, a_hi, a_lo, b_hi, b_lo, first, final):
                eng.matmul(dst, a_hi, b_hi, start=first, stop=False)
                eng.matmul(dst, a_hi, b_lo, start=False, stop=False)
                return eng.matmul(dst, a_lo, b_hi, start=False, stop=final)

            def cols(kind, j):
                wide = 2 if kind == SR else 1
                return (lambda c: W1[kind] + wide * c + j // HC), bass.ts(j % HC, P)

            def layer1(kind, j):
                at, n = cols(kind, j)
                dst = bank[hidden_bank(kind, j)][:, :]
                for c in range(HC):
                    last = product(dst, w_hi[:, at(c), n], w_lo[:, at(c), n], x_hi[:, c, :], x_lo[:, c, :], c == 0, c == HC - 1)
                last.then_inc(s_h, 1)

            def layer2_sr(j, i, final=False):
                last = product(bank[i][:, :], w_hi[:, W2[SR] + j, bass.ts(i, P)], w_lo[:, W2[SR] + j, bass.ts(i, P)], g_hi[:, j % 4, :], g_lo[:, j % 4, :], j == 0, j == 7)
                if final:
                    last.then_inc(s_h, 1)

            def last_layer(w, j, t):
                n = bass.ts(t, P)
                if j == 0:
                    pass
                last = product(bank[4 + t][:, :], g_hi[:, j, n], g_lo[:, j, n], w_hi[:, w + j, :], w_lo[:, w + j, :], j == 0, j == HC - 1)
                if j == HC - 1:
                    last.then_inc(s_y, 1)

            def body(kind):
                for f in range(2):
                    take(eng, s_xs)
                    eng.sem_inc(s_stage, 1)
                if kind == NONE:
                    return
                eng.wait_ge(s_wsplit, 2 + {NR: 4, TSR: 8, SR: 18}[kind])
                if kind != SR:
                    for j in range(HC):
                        layer1(kind, j)
                    for j in range(HC):
                        take(eng, s_gs)
                        for t in range(TT):
                            if j == 0:
                                take(eng, s_acc)
                            last_layer(W2[kind], j, t)
                    return
                for j in range(4):
                    if j == 2:
                        take(eng, s_acc, 4)
                    layer1(kind, j)
                for j in range(6):
                    take(eng, s_gs)
                    for i in range(HC):
                        if j == 0 and i == 2:
                            take(eng, s_gs)
                        layer2_sr(j, i)
                    if j + 4 < 8:
                        layer1(kind, j + 4)
                    if j == 0:
                        eng.sem_inc(s_gs, 1)
                take(eng, s_gs, 2)
                for i in range(HC):
                    layer2_sr(6, i)
                    layer2_sr(7, i, final=True)
                for j in range(HC):
                    take(eng, s_gs)
                    for t in range(TT):
                        last_layer(W3[SR], j, t)

            eng.wait_ge(s_const, 48)
            eng.sem_inc(s_acc, 4)
            over_batches(eng, lambda b, last: dispatch(eng, b, body))

        @block.scalar
        def _(eng):
            def hi_half(f, dst):
                take(eng, s_full[f], 16)
                eng.copy(dst, stage[:, f, :, :]).then_inc(s_hi, 1)

            def split_x():
                for f in range(2):
                    hi_half(f, x_hi[:, 2 * f:2 * f + 2, :])

            def gelu(psum, slot, col, landed=1):
                if landed:
                    take(eng, s_h, landed)
                b = bcol[:, col:col + 1]
                eng.activation(g_hi[:, slot, :], psum, ACT.Gelu, bias=b)
                eng.activation(psum, psum, ACT.Gelu, bias=b).then_inc(s_g, 1)

            def step(b, last):
                def body(kind):
                    if kind != NONE:
                        for j in range(8 if kind == SR else 4):
                            gelu(bank[hidden_bank(kind, j)][:, :], j % 4, B1[kind] + j)
                    if not last:
                        split_x()
                    if kind == SR:
                        for i in range(HC):
                            gelu(bank[i][:, :], i, B2[SR] + i, (1, 1, 2, 0)[i])

                dispatch(eng, b, body)
                for t in range(TT):
                    if t % 2 == 0:
                        take(eng, s_rstd)
                    take(eng, s_v)
                    eng.activation(y[:, t, :], y[:, t, :], ACT.Copy, scale=rstd[:, t:t + 1]).then_inc(s_n, 1)

            split_x()
            eng.wait_ge(s_const, 48)
            for u in range(N_WCHUNK // 2):
                hi_half(u % 2, w_hi[:, 2 * u:2 * u + 2, :])
            over_batches(eng, step)

        @block.vector
        def _(eng):
            def lo_half(f, dst, hi):
                take(eng, s_hi)
                return eng.tensor_tensor(dst, stage[:, f, :, :], hi, ALU.subtract)

            def split_x(count):
                for f in range(2):
                    h = slice(2 * f, 2 * f + 2)
                    lo_half(f, x_lo[:, h, :], x_hi32[:, h, :]).then_inc(s_xs, 1)

            def lo_chunk(psum, slot):
                take(eng, s_g)
                eng.tensor_tensor(g_lo[:, slot, :], psum, g_hi32[:, slot, :], ALU.subtract).then_inc(s_gs, 1)

            def step(b, last):
                def body(kind):
                    if kind != NONE:
                        for j in range(8 if kind == SR else 4):
                            lo_chunk(bank[hidden_bank(kind, j)][:, :], j % 4)
                    if not last:
                        split_x(1)
                    if kind == SR:
                        for i in range(HC):
                            lo_chunk(bank[i][:, :], i)
                    for t in range(TT):
                        take(eng, s_xb)
                        if kind != NONE:
                            take(eng, s_y)
                            eng.tensor_tensor(y[:, t, :], bank[4 + t][:, :], y[:, t, :], ALU.add).then_inc(s_ev, 1)
                    if kind != NONE:
                        take(eng, s_ev, TT)
                        eng.sem_inc(s_acc, TT)

                dispatch(eng, b, body)
                for t in range(TT):
                    eng.bn_stats(bn[:, t, :], y[:, t, :]).then_inc(s_bn, 1)
                take(eng, s_bn, TT)
                for t in range(TT):
                    eng.bn_aggr(mv[:, t, :], bn[:, t, :]).then_inc(s_mv, 1)
                take(eng, s_mv, TT)
                eng.sem_inc(s_var, TT)
                for t in range(TT):
                    eng.scalar_tensor_tensor(out=y[:, t, :], in0=y[:, t, :], scalar=mv[:, t, 0:1], in1=row[:, R_GAMMA, :],
                                             op0=ALU.subtract, op1=ALU.mult).then_inc(s_v, 1)

            for f in range(2):
                h = slice(2 * f, 2 * f + 2)
                lo_half(f, x_lo[:, h, :], x_hi32[:, h, :]).then_inc(s_wsplit, 1)
            eng.wait_ge(s_wsplit, 2)
            eng.sem_inc(s_xs, 2)
            for u in range(N_WCHUNK // 2):
                c = slice(2 * u, 2 * u + 2)
                lo_half(u % 2, w_lo[:, c, :], w_hi32[:, c, :]).then_inc(s_wsplit, 1)
            eng.wait_ge(s_const, 48)
            over_batches(eng, step)

        @block.gpsimd
        def _(eng):
            eng.memset(power[:, :], -0.5).then_inc(s_power, 1)
            eng.wait_ge(s_power, 1)
            eng.wait_ge(s_const, 48)

            def step(b, last):
                def body(kind):
                    for t in range(TT):
                        if t % 2 == 0:
                            take(eng, s_row[t // 2], 16)
                        if kind == NONE:
                            eng.sem_inc(s_xb, 1)
                        else:
                            eng.tensor_tensor(y[:, t, :], y[:, t, :], row[:, kind, :], ALU.add).then_inc(s_xb, 1)

                dispatch(eng, b, body)
                take(eng, s_var, TT)
                eng.tensor_scalar(var_eps[:, :], mv[:, :, 1], EPS, None, ALU.add).then_inc(s_eps, 1)
                take(eng, s_eps)
                eng.tensor_tensor(rstd[:, :], var_eps[:, :], power[:, :], ALU.pow).then_inc(s_rstd, 2)
                for t in range(TT):
                    take(eng, s_n)
                    eng.tensor_tensor(y[:, t, :], y[:, t, :], row[:, R_BETA, :], ALU.add).then_inc(s_fin, 1)

            over_batches(eng, step)


def kernel(x, itok_B_0_2, L0_cond_w1_nr, L0_cond_b1_nr, L0_cond_w2_nr, L0_cond_b2_nr, L0_cond_w1_tsr, L0_cond_b1_tsr,
           L0_cond_w2_tsr, L0_cond_b2_tsr, L0_cond_w1_sr, L0_cond_b1_sr, L0_cond_w2_sr, L0_cond_b2_sr, L0_cond_w3_sr,
           L0_cond_b3_sr, L0_cond_gamma, L0_cond_beta):
    import numpy as np
    import concourse.bacc as bacc
    from concourse.bass_utils import run_bass_kernel_spmd

    x = np.ascontiguousarray(x)

    def by_column(w):
        h, n = w.shape
        return np.asarray(w).reshape(P, HC, n // H, H).transpose(1, 2, 0, 3).reshape(-1, P, H)

    def by_chunk(w):
        return np.asarray(w).reshape(-1, P, H)

    chunks = np.concatenate([
        by_column(L0_cond_w1_nr), by_chunk(L0_cond_w2_nr), by_column(L0_cond_w1_tsr), by_chunk(L0_cond_w2_tsr),
        by_column(L0_cond_w1_sr), by_chunk(L0_cond_w2_sr), by_chunk(L0_cond_w3_sr)])
    arrays = {
        "x": x,
        "x_t": np.ascontiguousarray(
            x.reshape(NBATCH, P, TT, P, HC).transpose(0, 4, 3, 2, 1).reshape(NBATCH, 2, 2, P, T).transpose(0, 1, 3, 2, 4)
        ).reshape(NBATCH, 2, P, 2 * T),
        "cond": np.ascontiguousarray(itok_B_0_2),
        "weights": np.ascontiguousarray(chunks.reshape(N_WCHUNK // 2, 2, P, H).transpose(0, 2, 1, 3)).reshape(-1, P, 2 * H),
        "bias_cols": np.ascontiguousarray(np.concatenate([
            np.asarray(L0_cond_b1_nr), np.asarray(L0_cond_b1_tsr), np.asarray(L0_cond_b1_sr), np.asarray(L0_cond_b2_sr)]).reshape(N_BCOL, P).T),
        "rows": np.stack([np.asarray(a) for a in (L0_cond_b2_nr, L0_cond_b2_tsr, L0_cond_b3_sr, L0_cond_gamma, L0_cond_beta)]),
    }
    nc = bacc.Bacc("TRN2", target_bir_lowering=False, num_devices=1)
    args = [nc.dram_tensor(n, a.shape, mybir.dt.from_np(a.dtype), kind="ExternalInput").ap() for n, a in arrays.items()]
    out = nc.dram_tensor("out", x.shape, mybir.dt.float32, kind="ExternalOutput").ap()
    conditional_mlp(nc, *args, out)
    result = run_bass_kernel_spmd(nc, [arrays], core_ids=[0])
    return result.results[0]["out"]
```

```python
from contextlib import ExitStack

import concourse.bass as bass
from concourse import mybir

P = 128
NBATCH = 16
T = 512
H = 512
HC = H // P
TT = T // P
EPS = 1e-5
NR, TSR, SR, NONE = 0, 1, 2, 3

W1, W2, W3 = {NR: 0, SR: 8, TSR: 28}, {NR: 4, SR: 16, TSR: 32}, {SR: 24}
N_WCHUNK = 36
B1, B2 = {NR: 0, TSR: 4, SR: 8}, {SR: 16}
N_BCOL = 20
R_GAMMA, R_BETA, N_ROW = 3, 4, 5


ITEMS = [("x", 0), ("w", 0), ("x", 1)] + [("w", u) for u in range(1, N_WCHUNK // 2)]
SLOTS = [0, 1, 2, 3, 4, 0, 1, 2, 3, 4] + [0, 1, 2] * 3 + [0]
N_ITEM = len(ITEMS)
Y_ITEMS = 10
NEEDS = {NR: ITEMS.index(("w", 3)) + 1, SR: ITEMS.index(("w", 13)) + 1, TSR: N_ITEM, NONE: N_ITEM}
WOVEN = {NR: (1, 2, 2, 3, 3), SR: (0, 1, 1, 1), TSR: (), NONE: ()}


def item_before(i):
    before = [n for n in range(i) if SLOTS[n] == SLOTS[i]]
    return before[-1] if before else None


def conditional_mlp(nc, x, x_t, cond, weights, bias_cols, rows, out):
    fp32, fp32r, i32 = mybir.dt.float32, mybir.dt.float32r, mybir.dt.int32
    ALU, ACT = mybir.AluOpType, mybir.ActivationFunctionType
    ctx = ExitStack()
    with ctx:
        def sb(name, shape, dt=fp32):
            return ctx.enter_context(nc.sbuf_tensor(name, shape, dt))

        def sem(name):
            return ctx.enter_context(nc.semaphore(name))

        w_hi = sb("w_hi", [P, N_WCHUNK, H], fp32r)
        w_lo = sb("w_lo", [P, N_WCHUNK, H], fp32r)
        stage = sb("stage", [P, 3, 2, T])
        x_hi = sb("x_hi", [P, HC, T], fp32r)
        x_lo = sb("x_lo", [P, HC, T], fp32r)
        g_hi = sb("g_hi", [P, 4, T], fp32r)
        g_lo = sb("g_lo", [P, 4, T], fp32r)
        y = sb("y", [P, TT, H])
        row = sb("row", [P, N_ROW, H])
        bcol = sb("bcol", [P, N_BCOL])
        cond_sb = sb("cond_sb", [1, NBATCH], i32)
        bn = sb("bn", [P, TT, 6])
        mv = sb("mv", [P, TT, 2])
        var_eps = sb("var_eps", [P, TT])
        rstd = sb("rstd", [P, TT])
        power = sb("power", [P, TT])
        bank = [ctx.enter_context(nc.psum_tensor(f"bank{i}", [P, 512], fp32)) for i in range(8)]

        g_hi32 = g_hi[:, :, :].bitcast(fp32)
        x_hi32 = x_hi[:, :, :].bitcast(fp32)
        w_hi32 = w_hi[:, :, :].bitcast(fp32)

        s_const = sem("s_const")
        s_power = sem("s_power")
        s_full = [sem(f"s_full{i}") for i in range(5)]
        s_hi = sem("s_hi")
        s_item = sem("s_item")
        s_xs = sem("s_xs")
        s_stage = sem("s_stage")
        s_h = sem("s_h")
        s_g = sem("s_g")
        s_gs = sem("s_gs")
        s_y = sem("s_y")
        s_acc = sem("s_acc")
        s_row = [sem(f"s_row{t}") for t in range(TT)]
        s_xb = sem("s_xb")
        s_ev = sem("s_ev")
        s_bn = sem("s_bn")
        s_mv = sem("s_mv")
        s_var = sem("s_var")
        s_eps = sem("s_eps")
        s_rstd = sem("s_rstd")
        s_rstd_end = sem("s_rstd_end")
        s_v = sem("s_v")
        s_v_end = sem("s_v_end")
        s_n = sem("s_n")
        s_fin = sem("s_fin")
        s_out = [sem(f"s_out{t}") for t in range(TT)]

        def take(eng, s, n=1):
            eng.wait_ge(s, n)
            eng.sem_inc(s, -n)

        def dispatch(eng, b, body):
            c = eng.value_load(cond_sb[0:1, bass.ds(b, 1)])
            with eng.If(c == NR):
                body(NR)
            with eng.Else():
                with eng.If(c == SR):
                    body(SR)
                with eng.Else():
                    with eng.If(c == TSR):
                        body(TSR)
                    with eng.Else():
                        body(NONE)

        def over_batches(eng, step):
            step(0, True, False)
            with eng.Fori(1, NBATCH - 1) as b:
                step(b, False, False)
            step(NBATCH - 1, False, True)

        def slot(s):
            return stage[:, s, :, :] if s < 3 else y[:, 2 * (s - 3):2 * (s - 3) + 2, :]

        def n_hidden(kind):
            return {NR: 4, TSR: 4, SR: 8, NONE: 0}[kind]

        def hidden_bank(kind, j):
            if kind != SR:
                return j
            return (3, 2)[j] if j < 2 else 4 + (j - 2) % 4

        def first_items(kind, split):
            left = iter(range(NEEDS[NR], N_ITEM))
            for _ in range(NEEDS[kind] - NEEDS[NR]):
                split(next(left))

            def behind(j):
                for n in range(WOVEN[kind][j] if j < len(WOVEN[kind]) else 0):
                    split(next(left))
                if j == n_hidden(kind):
                    for i in left:
                        split(i)
            return behind

        block = ctx.enter_context(nc.Block())

        @block.sync
        def _(eng):
            x_rows = x.rearrange("b (p c) h -> b p c h", c=TT)
            out_rows = out.rearrange("b (p c) h -> b p c h", c=TT)
            x_halves = x_t.rearrange("b f p n -> (b f) p n")

            def load_slot(s, src):
                eng.dma_start(slot(s), src.rearrange("p (c n) -> p c n", c=2)).then_inc(s_full[s], 16)

            def tile_of(dram, b, t):
                return dram[bass.ds(b, 1), :, t, :].rearrange("a p h -> p (a h)")

            def store(b, t):
                take(eng, s_fin)
                eng.dma_start(tile_of(out_rows, b, t), y[:, t, :]).then_inc(s_out[t], 16)

            def load_row(b, t):
                eng.dma_start(y[:, t, :], tile_of(x_rows, b, t)).then_inc(s_row[t], 16)

            for i, (what, n) in enumerate(ITEMS):
                if item_before(i) is not None:
                    eng.wait_ge(s_item, item_before(i) + 1)
                load_slot(SLOTS[i], x_halves[n] if what == "x" else weights[n])
                if i == 4:
                    eng.dma_start(cond_sb[:, :], cond.rearrange("(a b) -> a b", a=1)).then_inc(s_const, 16)
                    eng.dma_start(bcol[:, :], bias_cols).then_inc(s_const, 16)
                    eng.dma_start(row[:, :, :], rows.rearrange("(a r) h -> a r h", a=1).to_broadcast([P, N_ROW, H])).then_inc(s_const, 16)
                if i == Y_ITEMS + 3:
                    eng.wait_ge(s_item, Y_ITEMS)
                    for t in range(TT):
                        load_row(0, t)
            for f in range(2):
                eng.wait_ge(s_item, max(n for n in range(N_ITEM) if SLOTS[n] == f) + 1)
                load_slot(f, x_halves[2 + f])

            def step(b, last=False):
                if not last:
                    for f in range(2):
                        take(eng, s_stage)
                        load_slot(f, x_halves[bass.ds(b * 2 + (2 + f), 1), :, :].rearrange("a p n -> p (a n)"))

                def reload(t):
                    take(eng, s_out[t], 16)
                    load_row(b, t)

                for t in range(TT):
                    store(b - 1, t)
                    if t >= 2:
                        reload(t - 2)
                reload(2)
                reload(3)

            with eng.Fori(1, NBATCH - 1) as b:
                step(b)
            step(NBATCH - 1, True)
            for t in range(TT):
                store(NBATCH - 1, t)
            for t in range(TT):
                take(eng, s_out[t], 16)

        @block.tensor
        def _(eng):
            def product(dst, a_hi, a_lo, b_hi, b_lo, first, final):
                eng.matmul(dst, a_hi, b_hi, start=first, stop=False)
                eng.matmul(dst, a_hi, b_lo, start=False, stop=False)
                return eng.matmul(dst, a_lo, b_hi, start=False, stop=final)

            def layer1(kind, j, staged=False):
                dst, n = bank[hidden_bank(kind, j)][:, :], bass.ts(j % HC, P)
                wide = 2 if kind == SR else 1
                for c in range(HC):
                    if staged and c % 2 == 0:
                        eng.wait_ge(s_item, 2 + c)
                    w = W1[kind] + wide * c + j // HC
                    last = product(dst, w_hi[:, w, n], w_lo[:, w, n], x_hi[:, c, :], x_lo[:, c, :], c == 0, c == HC - 1)
                last.then_inc(s_h, 1)

            def layer2_sr(j, i):
                w, n = W2[SR] + j, bass.ts(i, P)
                return product(bank[i][:, :], w_hi[:, w, n], w_lo[:, w, n], g_hi[:, j % 4, :], g_lo[:, j % 4, :], j == 0, j == 7)

            def last_layer(w, claim):
                def add(j, t):
                    n = bass.ts(t, P)
                    return product(bank[4 + t][:, :], g_hi[:, j, n], g_lo[:, j, n], w_hi[:, w + j, :], w_lo[:, w + j, :], j == 0, j == HC - 1)

                for j in range(2):
                    take(eng, s_gs)
                    for t in range(TT):
                        if claim and j == 0:
                            take(eng, s_acc)
                        add(j, t)
                take(eng, s_gs, 2)
                for t in range(TT):
                    add(2, t)
                    add(3, t).then_inc(s_y, 1)

            def step(b, first, last):
                def body(kind):
                    if not first:
                        for f in range(2):
                            take(eng, s_xs)
                            eng.sem_inc(s_stage, 1)
                    if kind == NONE:
                        return
                    if not (first and kind == NR):
                        eng.wait_ge(s_item, NEEDS[kind])
                    if kind != SR:
                        for j in range(HC):
                            layer1(kind, j, staged=first and kind == NR and j == 0)
                        if first and kind == NR:
                            eng.wait_ge(s_item, NEEDS[NR])
                        last_layer(W2[kind], claim=True)
                        return
                    for j in range(4):
                        if j == 2:
                            take(eng, s_acc, 4)
                        layer1(kind, j)
                    for j in range(6):
                        if j != 1:
                            take(eng, s_gs)
                        for i in range(HC):
                            if j == 0 and i == 2:
                                take(eng, s_gs)
                            layer2_sr(j, i)
                        if j + 4 < 8:
                            layer1(kind, j + 4)
                    take(eng, s_gs, 2)
                    for i in range(HC):
                        layer2_sr(6, i)
                        layer2_sr(7, i).then_inc(s_h, 1)
                    last_layer(W3[SR], claim=False)

                dispatch(eng, b, body)

            eng.wait_ge(s_const, 48)
            eng.sem_inc(s_acc, 4)
            over_batches(eng, step)

        @block.scalar
        def _(eng):
            def hi_slot(s, dst):
                take(eng, s_full[s], 16)
                eng.copy(dst, slot(s)).then_inc(s_hi, 1)

            def split_item(i):
                what, n = ITEMS[i]
                hi_slot(SLOTS[i], (x_hi if what == "x" else w_hi)[:, 2 * n:2 * n + 2, :])

            def gelu(psum, slot, col, landed=1):
                if landed:
                    take(eng, s_h, landed)
                b = bcol[:, col:col + 1]
                eng.activation(g_hi[:, slot, :], psum, ACT.Gelu, bias=b)
                eng.activation(psum, psum, ACT.Gelu, bias=b).then_inc(s_g, 1)

            def step(b, first, last):
                def body(kind):
                    behind = first_items(kind, split_item) if first else None
                    for j in range(n_hidden(kind)):
                        gelu(bank[hidden_bank(kind, j)][:, :], j % 4, B1[kind] + j)
                        if first:
                            behind(j)
                    if first:
                        behind(n_hidden(kind))
                    if not last:
                        for f in range(2):
                            hi_slot(f, x_hi[:, 2 * f:2 * f + 2, :])
                    if kind == SR:
                        for i in range(HC):
                            gelu(bank[i][:, :], i, B2[SR] + i, (1, 1, 2, 0)[i])
                    if last:
                        return
                    for t in range(TT):
                        take(eng, s_v)
                        take(eng, s_rstd)
                        eng.activation(y[:, t, :], y[:, t, :], ACT.Copy, scale=rstd[:, t:t + 1]).then_inc(s_n, 1)

                dispatch(eng, b, body)

            for i in range(NEEDS[NR]):
                split_item(i)
            eng.wait_ge(s_const, 48)
            over_batches(eng, step)

        @block.vector
        def _(eng):
            def lo_slot(s, lo, hi32, c):
                take(eng, s_hi)
                return eng.tensor_tensor(lo[:, c, :], slot(s), hi32[:, c, :], ALU.subtract)

            def split_item(i):
                what, n = ITEMS[i]
                lo, hi32 = (x_lo, x_hi32) if what == "x" else (w_lo, w_hi32)
                lo_slot(SLOTS[i], lo, hi32, slice(2 * n, 2 * n + 2)).then_inc(s_item, 1)

            def lo_chunk(psum, slot):
                take(eng, s_g)
                eng.tensor_tensor(g_lo[:, slot, :], psum, g_hi32[:, slot, :], ALU.subtract).then_inc(s_gs, 1)

            def residual(kind, t):
                take(eng, s_xb)
                if kind != NONE:
                    take(eng, s_y)
                    eng.tensor_tensor(y[:, t, :], bank[4 + t][:, :], y[:, t, :], ALU.add).then_inc(s_ev, 1)

            def stats(kind, t):
                if kind != NONE:
                    take(eng, s_ev)
                    eng.sem_inc(s_acc, 1)
                eng.bn_stats(bn[:, t, :], y[:, t, :]).then_inc(s_bn, 1)

            def moments(kind, t):
                take(eng, s_bn)
                eng.bn_aggr(mv[:, t, :], bn[:, t, :]).then_inc(s_mv, 1)

            def centre(kind, t, done):
                take(eng, s_mv)
                eng.sem_inc(s_var, 1)
                eng.scalar_tensor_tensor(out=y[:, t, :], in0=y[:, t, :], scalar=mv[:, t, 0:1], in1=row[:, R_GAMMA, :],
                                         op0=ALU.subtract, op1=ALU.mult).then_inc(done, 1)

            def finish(t):
                take(eng, s_v_end)
                take(eng, s_rstd_end)
                eng.scalar_tensor_tensor(out=y[:, t, :], in0=y[:, t, :], scalar=rstd[:, t:t + 1], in1=row[:, R_BETA, :],
                                         op0=ALU.mult, op1=ALU.add).then_inc(s_fin, 1)

            def step(b, first, last):
                def body(kind):
                    behind = first_items(kind, split_item) if first else None
                    for j in range(n_hidden(kind)):
                        lo_chunk(bank[hidden_bank(kind, j)][:, :], j % 4)
                        if first:
                            behind(j)
                    if first:
                        behind(n_hidden(kind))
                    if not last:
                        for f in range(2):
                            lo_slot(f, x_lo, x_hi32, slice(2 * f, 2 * f + 2)).then_inc(s_xs, 1)
                    if kind == SR:
                        for i in range(HC):
                            lo_chunk(bank[i][:, :], i)
                    if last:
                        for t in range(TT + 1):
                            if t < TT:
                                residual(kind, t)
                            if t > 0:
                                finish_later = t - 1
                                centre(kind, finish_later, s_v_end)
                            if t < TT:
                                stats(kind, t)
                                moments(kind, t)
                            if t > 0:
                                finish(t - 1)
                        return
                    for t in range(0, TT, 2):
                        residual(kind, t)
                        residual(kind, t + 1)
                        stats(kind, t)
                        stats(kind, t + 1)
                        moments(kind, t)
                        moments(kind, t + 1)
                        centre(kind, t, s_v)
                        centre(kind, t + 1, s_v)

                dispatch(eng, b, body)

            for i in range(NEEDS[NR]):
                split_item(i)
            eng.wait_ge(s_const, 48)
            over_batches(eng, step)

        @block.gpsimd
        def _(eng):
            eng.memset(power[:, :], -0.5).then_inc(s_power, 1)
            eng.wait_ge(s_power, 1)
            eng.wait_ge(s_const, 48)

            def step(b, first, last):
                def body(kind):
                    for t in range(TT):
                        take(eng, s_row[t], 16)
                        if kind == NONE:
                            eng.sem_inc(s_xb, 1)
                        else:
                            eng.tensor_tensor(y[:, t, :], y[:, t, :], row[:, kind, :], ALU.add).then_inc(s_xb, 1)

                dispatch(eng, b, body)
                n = 1 if last else 2
                for t in range(0, TT, n):
                    take(eng, s_var, n)
                    eng.tensor_scalar(var_eps[:, t:t + n], mv[:, t:t + n, 1], EPS, None, ALU.add).then_inc(s_eps, 1)
                    take(eng, s_eps)
                    eng.tensor_tensor(rstd[:, t:t + n], var_eps[:, t:t + n], power[:, t:t + n], ALU.pow).then_inc(
                        s_rstd_end if last else s_rstd, n)
                if not last:
                    for t in range(TT):
                        take(eng, s_n)
                        eng.tensor_tensor(y[:, t, :], y[:, t, :], row[:, R_BETA, :], ALU.add).then_inc(s_fin, 1)

            over_batches(eng, step)


def kernel(x, itok_B_0_2, L0_cond_w1_nr, L0_cond_b1_nr, L0_cond_w2_nr, L0_cond_b2_nr, L0_cond_w1_tsr, L0_cond_b1_tsr,
           L0_cond_w2_tsr, L0_cond_b2_tsr, L0_cond_w1_sr, L0_cond_b1_sr, L0_cond_w2_sr, L0_cond_b2_sr, L0_cond_w3_sr,
           L0_cond_b3_sr, L0_cond_gamma, L0_cond_beta):
    import numpy as np
    import concourse.bacc as bacc
    from concourse.bass_utils import run_bass_kernel_spmd

    x = np.ascontiguousarray(x)

    def by_column(w):
        h, n = w.shape
        return np.asarray(w).reshape(P, HC, n // H, H).transpose(1, 2, 0, 3).reshape(-1, P, H)

    def by_chunk(w):
        return np.asarray(w).reshape(-1, P, H)

    chunks = np.concatenate([
        by_column(L0_cond_w1_nr), by_chunk(L0_cond_w2_nr), by_column(L0_cond_w1_sr), by_chunk(L0_cond_w2_sr),
        by_chunk(L0_cond_w3_sr), by_column(L0_cond_w1_tsr), by_chunk(L0_cond_w2_tsr)])
    arrays = {
        "x": x,
        "x_t": np.ascontiguousarray(
            x.reshape(NBATCH, P, TT, P, HC).transpose(0, 4, 3, 2, 1).reshape(NBATCH, 2, 2, P, T).transpose(0, 1, 3, 2, 4)
        ).reshape(NBATCH, 2, P, 2 * T),
        "cond": np.ascontiguousarray(itok_B_0_2),
        "weights": np.ascontiguousarray(chunks.reshape(N_WCHUNK // 2, 2, P, H).transpose(0, 2, 1, 3)).reshape(-1, P, 2 * H),
        "bias_cols": np.ascontiguousarray(np.concatenate([
            np.asarray(L0_cond_b1_nr), np.asarray(L0_cond_b1_tsr), np.asarray(L0_cond_b1_sr), np.asarray(L0_cond_b2_sr)]).reshape(N_BCOL, P).T),
        "rows": np.stack([np.asarray(a) for a in (L0_cond_b2_nr, L0_cond_b2_tsr, L0_cond_b3_sr, L0_cond_gamma, L0_cond_beta)]),
    }
    nc = bacc.Bacc("TRN2", target_bir_lowering=False, num_devices=1)
    args = [nc.dram_tensor(n, a.shape, mybir.dt.from_np(a.dtype), kind="ExternalInput").ap() for n, a in arrays.items()]
    out = nc.dram_tensor("out", x.shape, mybir.dt.float32, kind="ExternalOutput").ap()
    conditional_mlp(nc, *args, out)
    result = run_bass_kernel_spmd(nc, [arrays], core_ids=[0])
    return result.results[0]["out"]
```

```python
from contextlib import ExitStack

import concourse.bass as bass
from concourse import mybir

P = 128
NBATCH = 16
T = 512
H = 512
HC = H // P
TT = T // P
EPS = 1e-5
NR, TSR, SR, NONE = 0, 1, 2, 3

W1, W2, W3 = {NR: 0, SR: 8, TSR: 28}, {NR: 4, SR: 16, TSR: 32}, {SR: 24}
N_WCHUNK = 36
B1, B2 = {NR: 0, TSR: 4, SR: 8}, {SR: 16}
N_BCOL = 20
R_GAMMA, R_BETA, N_ROW = 3, 4, 5

PAIRS = {"nr": 0, "sr": 4, "sr2": 8, "sr3": 12, "tsr": 14}
EARLY = [("x0", 0), ("nr", 0), ("x0", 1), ("nr", 1), ("nr", 2), ("nr", 3),
         ("sr", 0), ("sr", 1), ("sr", 2), ("sr", 3)]
EARLY_SLOTS = [0, 1, 2, 3, 4, 0, 1, 2, 3, 4]
N_PROLOGUE = 6
PIECES = [(EARLY[i], c) for c in range(2) for i in range(2)]
SR2 = [("sr2", n) for n in range(4)]
X1 = [("x1", 0), ("x1", 1)]
LATE = [("sr3", 0), ("sr3", 1)] + [("tsr", n) for n in range(4)]


def by_gpsimd(kind):
    return SR2[2:] + LATE if kind == NR else LATE


def late_loads(kind):
    rest = list(zip(SR2 + LATE, [2, 0, 1, 2] + [0, 1, 2, 0, 1, 2]))
    x1 = list(zip(X1, [0, 1]))
    return x1 + rest if kind == NR else rest + x1


ORDER = [(j, t) for j in range(2) for t in range(TT)] + [(j, t) for t in range(TT) for j in (2, 3)]
ORDER_END = ([(0, 0), (0, 1), (1, 0), (1, 1), (2, 0), (3, 0), (2, 1), (3, 1)] +
             [(j, t) for t in (2, 3) for j in range(4)])
FINISHED_BY_VECTOR = 2
VECTOR_END = [("residual", 0), ("stats", 0), ("residual", 1), ("moments", 0), ("stats", 1), ("centre", 0),
              ("moments", 1), ("residual", 2), ("centre", 1), ("stats", 2), ("moments", 2), ("residual", 3),
              ("centre", 2), ("stats", 3), ("moments", 3), ("centre", 3), ("finish", 2), ("finish", 3)]
GPSIMD_END = [("deviation", 0), ("deviation", 1), ("shift", 0), ("deviation", 2), ("shift", 1), ("deviation", 3)]
N_WARM = 10


def conditional_mlp(nc, x, x_t, cond, weights, bias_cols, rows, out):
    fp32, fp32r, i32 = mybir.dt.float32, mybir.dt.float32r, mybir.dt.int32
    ALU, ACT = mybir.AluOpType, mybir.ActivationFunctionType
    ctx = ExitStack()
    with ctx:
        def sb(name, shape, dt=fp32):
            return ctx.enter_context(nc.sbuf_tensor(name, shape, dt))

        def sem(name):
            return ctx.enter_context(nc.semaphore(name))

        w_hi = sb("w_hi", [P, N_WCHUNK, H], fp32r)
        w_lo = sb("w_lo", [P, N_WCHUNK, H], fp32r)
        stage = sb("stage", [P, 3, 2, T])
        x_hi = sb("x_hi", [P, HC, T], fp32r)
        x_lo = sb("x_lo", [P, HC, T], fp32r)
        g_hi = sb("g_hi", [P, 4, T], fp32r)
        g_lo = sb("g_lo", [P, 4, T], fp32r)
        y = sb("y", [P, TT, H])
        row = sb("row", [P, N_ROW, H])
        bcol = sb("bcol", [P, N_BCOL])
        cond_sb = sb("cond_sb", [1, NBATCH], i32)
        bn = sb("bn", [P, TT, 6])
        mv = sb("mv", [P, TT, 2])
        var_eps = sb("var_eps", [P, TT])
        rstd = sb("rstd", [P, TT])
        power = sb("power", [P, TT])
        unused = sb("unused", [1, 1])
        bank = [ctx.enter_context(nc.psum_tensor(f"bank{i}", [P, 512], fp32)) for i in range(8)]

        g_hi32 = g_hi[:, :, :].bitcast(fp32)
        zeros = g_hi[:, :, :].bitcast(mybir.dt.bfloat16)[:, 0, 0:512]
        x_hi32 = x_hi[:, :, :].bitcast(fp32)
        w_hi32 = w_hi[:, :, :].bitcast(fp32)

        s_const = sem("s_const")
        s_cond = sem("s_cond")
        s_row0 = sem("s_row0")
        s_rows = sem("s_rows")
        s_power = sem("s_power")
        s_full = [sem(f"s_full{i}") for i in range(5)]
        s_loaded = {item: sem(f"s_loaded_{item[0]}_{item[1]}") for item in by_gpsimd(NR)}
        s_piece = [sem(f"s_piece{i}") for i in range(len(PIECES))]
        s_zero = sem("s_zero")
        s_first = sem("s_first")
        s_hi = sem("s_hi")
        s_split = {g: sem(f"s_split_{g}") for g in ("x0", "x1", "nr", "sr", "sr3", "tsr")}
        s_split_sr2 = {item: sem(f"s_split_sr2_{item[1]}") for item in SR2}
        s_xs = sem("s_xs")
        s_stage = sem("s_stage")
        s_h = sem("s_h")
        s_g = sem("s_g")
        s_gs = sem("s_gs")
        s_y = sem("s_y")
        s_acc = sem("s_acc")
        s_row = [sem(f"s_x_row{t}") for t in range(TT)]
        s_xb = sem("s_xb")
        s_ev = sem("s_ev")
        s_bn = sem("s_bn")
        s_mv = sem("s_mv")
        s_var = sem("s_var")
        s_own = sem("s_own")
        s_rstd = sem("s_rstd")
        s_rstd_end = sem("s_rstd_end")
        s_v = sem("s_v")
        s_v_end = sem("s_v_end")
        s_n = sem("s_n")
        s_fin = sem("s_fin")
        s_fin_end = sem("s_fin_end")
        s_out = [sem(f"s_out{t}") for t in range(TT)]

        def take(eng, s, n=1):
            eng.wait_ge(s, n)
            eng.sem_inc(s, -n)

        def split_done(item):
            return s_split_sr2[item] if item in SR2 else s_split[item[0]]

        def wait_split(eng, item):
            eng.wait_ge(split_done(item), 1 if item in SR2 else item[1] + 1)

        def dispatch(eng, c, body):
            with eng.If_cmp(c, NR, "IS_EQ"):
                body(NR)
            with eng.Else():
                with eng.If_cmp(c, SR, "IS_EQ"):
                    body(SR)
                with eng.Else():
                    with eng.If_cmp(c, TSR, "IS_EQ"):
                        body(TSR)
                    with eng.Else():
                        body(NONE)

        def over_batches(eng, step):
            eng.wait_ge(s_cond, 16)
            c = eng.alloc_register(f"condition_{eng.engine.name}")
            eng.reg_load(c, cond_sb[0:1, 0:1])

            def run(b, first, last):
                def read_next():
                    if not last:
                        eng.reg_load(c, cond_sb[0:1, bass.ds(b + 1, 1)])

                dispatch(eng, c, step(read_next, first, last))

            run(0, True, False)
            with eng.Fori(1, NBATCH - 1) as b:
                run(b, False, False)
            run(NBATCH - 1, False, True)

        def slot(s):
            return stage[:, s, :, :] if s < 3 else y[:, 2 * (s - 3):2 * (s - 3) + 2, :]

        def n_hidden(kind):
            return {NR: 4, TSR: 4, SR: 8, NONE: 0}[kind]

        def hidden_bank(kind, j):
            if kind != SR:
                return j
            return (3, 2)[j] if j < 2 else 4 + (j - 2) % 4

        def operand(item):
            group, n = item
            if group in PAIRS:
                n += PAIRS[group]
            c = slice(2 * n, 2 * n + 2)
            if group in PAIRS:
                return w_hi[:, c, :], w_lo[:, c, :], w_hi32[:, c, :]
            return x_hi[:, c, :], x_lo[:, c, :], x_hi32[:, c, :]

        def slot_of(kind):
            return {**dict(zip(EARLY, EARLY_SLOTS)), **dict(late_loads(kind))}

        block = ctx.enter_context(nc.Block())

        @block.sync
        def _(eng):
            x_rows = x.rearrange("b (p c) h -> b p c h", c=TT)
            out_rows = out.rearrange("b (p c) h -> b p c h", c=TT)
            x_halves = x_t.rearrange("b f p n -> (b f) p n")

            def load_slot(s, src, full=None):
                eng.dma_start(slot(s), src.rearrange("p (c n) -> p c n", c=2)).then_inc(full or s_full[s], 16)

            def tile_of(dram, b, t):
                return dram[bass.ds(b, 1), :, t, :].rearrange("a p h -> p (a h)")

            def store(b, t, finished=s_fin):
                take(eng, finished)
                eng.dma_start(tile_of(out_rows, b, t), y[:, t, :]).then_inc(s_out[t], 16)

            def load_row(b, t):
                eng.dma_start(y[:, t, :], tile_of(x_rows, b, t)).then_inc(s_row[t], 16)

            def load_item(item, s, former, full=None):
                group, n = item
                if former:
                    wait_split(eng, former)
                load_slot(s, weights[PAIRS[group] + n] if group in PAIRS else x_halves[n + (2 if group == "x1" else 0)], full)

            for i, ((group, _), c) in enumerate(PIECES):
                src = (x_halves if group == "x0" else weights)[0]
                eng.dma_start(slot(EARLY.index(PIECES[i][0]))[:, c, :], src[:, c * T:(c + 1) * T]).then_inc(s_piece[i], 16)
                if i == 1:
                    eng.dma_start(cond_sb[:, :], cond.rearrange("(a b) -> a b", a=1)).then_inc(s_cond, 16)
            in_slot = {}
            for i, (item, s) in enumerate(zip(EARLY, EARLY_SLOTS)):
                if i >= 2:
                    load_item(item, s, in_slot.get(s))
                in_slot[s] = item
                if i == 3:
                    eng.dma_start(bcol[:, :], bias_cols).then_inc(s_const, 16)
                    eng.dma_start(row[0:1, :, :], rows.rearrange("(a r) h -> a r h", a=1)).then_inc(s_row0, 16)

            def body(kind):
                held = dict(in_slot)
                for i, (item, s) in enumerate(late_loads(kind)):
                    if i == 2:
                        for t in range(TT):
                            if t % 2 == 0:
                                wait_split(eng, in_slot[3 + t // 2])
                            load_row(0, t)
                    load_item(item, s, held[s], s_loaded[item] if item in by_gpsimd(kind) else None)
                    held[s] = item
                for f in range(2):
                    wait_split(eng, held[f])

            eng.wait_ge(s_cond, 16)
            c = eng.alloc_register("condition_SP")
            eng.reg_load(c, cond_sb[0:1, 0:1])
            dispatch(eng, c, body)

            def step(b, last=False):
                if not last:
                    for f in range(2):
                        take(eng, s_stage)
                        load_slot(f, x_halves[bass.ds(b * 2 + (2 + f), 1), :, :].rearrange("a p n -> p (a n)"))

                def reload(t):
                    take(eng, s_out[t], 16)
                    load_row(b, t)

                for t in range(TT):
                    store(b - 1, t)
                    if t >= 2:
                        reload(t - 2)
                reload(2)
                reload(3)

            with eng.Fori(1, NBATCH - 1) as b:
                step(b)
            step(NBATCH - 1, True)
            for t in range(TT):
                store(NBATCH - 1, t, s_fin if t < FINISHED_BY_VECTOR else s_fin_end)
            for t in range(TT):
                take(eng, s_out[t], 16)

        @block.tensor
        def _(eng):
            def product(dst, a_hi, a_lo, b_hi, b_lo, first, final):
                eng.matmul(dst, a_hi, b_hi, start=first, stop=False)
                eng.matmul(dst, a_hi, b_lo, start=False, stop=False)
                return eng.matmul(dst, a_lo, b_hi, start=False, stop=final)

            def layer1(kind, j, chunks=range(HC)):
                dst, n = bank[hidden_bank(kind, j)][:, :], bass.ts(j % HC, P)
                wide = 2 if kind == SR else 1
                for c in chunks:
                    w = W1[kind] + wide * c + j // HC
                    last = product(dst, w_hi[:, w, n], w_lo[:, w, n], x_hi[:, c, :], x_lo[:, c, :], c == 0, c == HC - 1)
                if c == HC - 1:
                    last.then_inc(s_h, 1)

            def layer1_staged():
                eng.wait_ge(s_first, 2)
                for chunks in ([0], [1], [2, 3]):
                    if chunks != [0]:
                        eng.wait_ge(s_split["x0"], chunks[0] // 2 + 1)
                        eng.wait_ge(s_split["nr"], chunks[0] // 2 + 1)
                    for j in range(HC):
                        layer1(NR, j, chunks)

            def layer2_sr(j, i):
                w, n = W2[SR] + j, bass.ts(i, P)
                return product(bank[i][:, :], w_hi[:, w, n], w_lo[:, w, n], g_hi[:, j % 4, :], g_lo[:, j % 4, :], j == 0, j == 7)

            def last_layer(w, claim, last):
                def add(j, t):
                    n = bass.ts(t, P)
                    return product(bank[4 + t][:, :], g_hi[:, j, n], g_lo[:, j, n], w_hi[:, w + j, :], w_lo[:, w + j, :], j == 0, j == HC - 1)

                seen = 0
                for j, t in ORDER_END if last else ORDER:
                    if j == seen:
                        take(eng, s_gs)
                        seen += 1
                    if claim and j == 0:
                        take(eng, s_acc)
                    sums = add(j, t)
                    if j == HC - 1:
                        sums.then_inc(s_y, 1)

            def step(read_next, first, last):
                def body(kind):
                    def taken():
                        if not first:
                            eng.sem_inc(s_xs, -2)
                            eng.sem_inc(s_stage, 2)
                        read_next()

                    if not first:
                        eng.wait_ge(s_xs, 2)
                    if kind == NONE:
                        taken()
                        return
                    if kind == SR:
                        eng.wait_ge(s_split["sr"], 4)
                    if kind == TSR:
                        eng.wait_ge(s_split["tsr"], 4)
                    if first and kind != NR:
                        eng.wait_ge(s_split["x0"], 2)
                    if kind != SR:
                        if first and kind == NR:
                            taken()
                            layer1_staged()
                        else:
                            for j in range(HC):
                                layer1(kind, j)
                                if j == 0:
                                    taken()
                        if kind == NR:
                            eng.wait_ge(s_split["nr"], 4)
                        last_layer(W2[kind], claim=True, last=last)
                        return
                    for j in range(4):
                        if j == 2:
                            take(eng, s_acc, 4)
                        layer1(kind, j)
                        if j == 0:
                            taken()
                    for j in range(6):
                        if j % 2 == 0:
                            wait_split(eng, SR2[j // 2])
                        if j != 1:
                            take(eng, s_gs)
                        for i in range(HC):
                            if j == 0 and i == 2:
                                take(eng, s_gs)
                            layer2_sr(j, i)
                        if j + 4 < 8:
                            layer1(kind, j + 4)
                    wait_split(eng, SR2[3])
                    take(eng, s_gs, 2)
                    for i in range(HC):
                        layer2_sr(6, i)
                        layer2_sr(7, i).then_inc(s_h, 1)
                    eng.wait_ge(s_split["sr3"], 2)
                    last_layer(W3[SR], claim=False, last=last)

                return body

            eng.sem_inc(s_acc, 4)
            eng.wait_ge(s_zero, 1)
            for _ in range(N_WARM):
                eng.matmul(bank[7][:, :], zeros[:, 0:P], zeros, start=True, stop=True)
            over_batches(eng, step)

        @block.scalar
        def _(eng):
            def hi_slot(s, dst):
                take(eng, s_full[s], 16)
                eng.copy(dst, slot(s)).then_inc(s_hi, 1)

            def split_item(item, s):
                hi_slot(s, operand(item)[0])

            def gelu(psum, slot, col, landed=1):
                if landed:
                    take(eng, s_h, landed)
                b = bcol[:, col:col + 1]
                eng.activation(g_hi[:, slot, :], psum, ACT.Gelu, bias=b)
                eng.activation(psum, psum, ACT.Gelu, bias=b).then_inc(s_g, 1)

            def step(read_next, first, last):
                def body(kind):
                    def split(items):
                        for item in items if first else []:
                            split_item(item, slot_of(kind)[item])

                    read_next()
                    split(EARLY[6:7] if kind == NR else EARLY[6:] + SR2)
                    for j in range(n_hidden(kind)):
                        gelu(bank[hidden_bank(kind, j)][:, :], j % 4, B1[kind] + j)
                        if kind == NR:
                            split((EARLY[7:9], EARLY[9:10], [], [])[j])
                    if kind == SR:
                        for i in range(HC):
                            gelu(bank[i][:, :], i, B2[SR] + i, (1, 1, 2, 0)[i])
                    split(X1)
                    if not first and not last:
                        for f in range(2):
                            hi_slot(f, x_hi[:, 2 * f:2 * f + 2, :])
                    if kind == NR:
                        split(SR2[:2])
                    for t in range(FINISHED_BY_VECTOR if last else TT):
                        take(eng, s_v)
                        take(eng, s_rstd)
                        eng.activation(y[:, t, :], y[:, t, :], ACT.Copy, scale=rstd[:, t:t + 1]).then_inc(s_n, 1)

                return body

            eng.wait_ge(s_power, 1)
            eng.activation(unused[0:1, :], power[0:1, 0:1], ACT.Gelu)
            for i, (item, c) in enumerate(PIECES):
                take(eng, s_piece[i], 16)
                eng.copy(operand(item)[0][:, c, :], slot(EARLY.index(item))[:, c, :]).then_inc(s_hi, 1)
            for item, s in zip(EARLY[2:N_PROLOGUE], EARLY_SLOTS[2:]):
                split_item(item, s)
            eng.wait_ge(s_const, 16)
            over_batches(eng, step)

        @block.vector
        def _(eng):
            def lo_slot(s, lo, hi32):
                take(eng, s_hi)
                return eng.tensor_tensor(lo, slot(s), hi32, ALU.subtract)

            def split_item(item, s):
                _, lo, hi32 = operand(item)
                lo_slot(s, lo, hi32).then_inc(split_done(item), 1)

            def lo_chunk(psum, slot):
                take(eng, s_g)
                eng.tensor_tensor(g_lo[:, slot, :], psum, g_hi32[:, slot, :], ALU.subtract).then_inc(s_gs, 1)

            def residual(kind, t):
                take(eng, s_xb)
                if kind != NONE:
                    take(eng, s_y)
                    eng.tensor_tensor(y[:, t, :], bank[4 + t][:, :], y[:, t, :], ALU.add).then_inc(s_ev, 1)

            def stats(kind, t):
                if kind != NONE:
                    take(eng, s_ev)
                    eng.sem_inc(s_acc, 1)
                eng.bn_stats(bn[:, t, :], y[:, t, :]).then_inc(s_bn, 1)

            def moments(kind, t):
                take(eng, s_bn)
                eng.bn_aggr(mv[:, t, :], bn[:, t, :]).then_inc(s_mv, 1)

            def centre(kind, t, done):
                take(eng, s_mv)
                eng.sem_inc(s_var, 1)
                eng.scalar_tensor_tensor(out=y[:, t, :], in0=y[:, t, :], scalar=mv[:, t, 0:1], in1=row[:, R_GAMMA, :],
                                         op0=ALU.subtract, op1=ALU.mult).then_inc(done, 1)

            def finish(kind, t):
                take(eng, s_v_end)
                take(eng, s_rstd_end)
                eng.scalar_tensor_tensor(out=y[:, t, :], in0=y[:, t, :], scalar=rstd[:, t:t + 1], in1=row[:, R_BETA, :],
                                         op0=ALU.mult, op1=ALU.add).then_inc(s_fin_end, 1)

            def step(read_next, first, last):
                def body(kind):
                    def split(items):
                        for item in items if first else []:
                            split_item(item, slot_of(kind)[item])

                    read_next()
                    split(EARLY[6:7] if kind == NR else EARLY[6:] + SR2)
                    for j in range(n_hidden(kind)):
                        lo_chunk(bank[hidden_bank(kind, j)][:, :], j % 4)
                        if kind == NR:
                            split((EARLY[7:9], EARLY[9:10], [], [])[j])
                    if kind == SR:
                        for i in range(HC):
                            lo_chunk(bank[i][:, :], i)
                    split(X1)
                    if first:
                        eng.wait_ge(s_split["x1"], 2)
                        eng.sem_inc(s_xs, 2)
                    elif not last:
                        for f in range(2):
                            c = slice(2 * f, 2 * f + 2)
                            lo_slot(f, x_lo[:, c, :], x_hi32[:, c, :]).then_inc(s_xs, 1)
                    if first:
                        eng.wait_ge(s_rows, 1)
                    if last:
                        def centre_end(kind, t):
                            centre(kind, t, s_v if t < FINISHED_BY_VECTOR else s_v_end)

                        do = {"residual": residual, "stats": stats, "moments": moments, "centre": centre_end,
                              "finish": finish}
                        for name, t in VECTOR_END:
                            do[name](kind, t)
                        return
                    if first and kind == NR:
                        for part in (residual, stats, moments):
                            for t in range(TT):
                                part(kind, t)
                        for t in range(TT):
                            centre(kind, t, s_v)
                        split(SR2[:2])
                        return
                    for t in range(0, TT, 2):
                        residual(kind, t)
                        residual(kind, t + 1)
                        stats(kind, t)
                        stats(kind, t + 1)
                        moments(kind, t)
                        moments(kind, t + 1)
                        centre(kind, t, s_v)
                        centre(kind, t + 1, s_v)

                return body

            eng.memset(zeros, 0.0).then_inc(s_zero, 1)
            for item, c in PIECES:
                _, lo, hi32 = operand(item)
                take(eng, s_hi)
                eng.tensor_tensor(lo[:, c, :], slot(EARLY.index(item))[:, c, :], hi32[:, c, :],
                                  ALU.subtract).then_inc(s_first if c == 0 else s_split[item[0]], 1)
            for item, s in zip(EARLY[2:N_PROLOGUE], EARLY_SLOTS[2:]):
                split_item(item, s)
            over_batches(eng, step)

        @block.gpsimd
        def _(eng):
            eng.memset(power[:, :], -0.5).then_inc(s_power, 1)
            eng.wait_ge(s_power, 1)
            eng.wait_ge(s_row0, 16)
            eng.partition_broadcast(row[:, :, :].rearrange("p r h -> p (r h)"), row[0:1, :, :].rearrange("p r h -> p (r h)"),
                                    P).then_inc(s_rows, 1)
            eng.wait_ge(s_rows, 1)

            def step(read_next, first, last):
                def body(kind):
                    read_next()

                    def split_items():
                        for item in by_gpsimd(kind):
                            hi, lo, hi32 = operand(item)
                            s = slot_of(kind)[item]
                            eng.wait_ge(s_loaded[item], 16)
                            eng.tensor_scalar(hi, slot(s), 1.0, 0.0, ALU.mult, ALU.add).then_inc(s_own, 1)
                            take(eng, s_own)
                            eng.tensor_tensor(lo, slot(s), hi32, ALU.subtract).then_inc(split_done(item), 1)

                    for t in range(TT):
                        take(eng, s_row[t], 16)
                        if kind == NONE:
                            eng.sem_inc(s_xb, 1)
                        else:
                            eng.tensor_tensor(y[:, t, :], y[:, t, :], row[:, kind, :], ALU.add).then_inc(s_xb, 1)
                    if first and kind != NR:
                        split_items()

                    def deviations(t, n, done):
                        take(eng, s_var, n)
                        eng.tensor_scalar(var_eps[:, t:t + n], mv[:, t:t + n, 1], EPS, None, ALU.add).then_inc(s_own, 1)
                        take(eng, s_own)
                        eng.tensor_tensor(rstd[:, t:t + n], var_eps[:, t:t + n], power[:, t:t + n], ALU.pow).then_inc(done, n)

                    def shift(t):
                        take(eng, s_n)
                        eng.tensor_tensor(y[:, t, :], y[:, t, :], row[:, R_BETA, :], ALU.add).then_inc(s_fin, 1)

                    if last:
                        for name, t in GPSIMD_END:
                            if name == "deviation":
                                deviations(t, 1, s_rstd if t < FINISHED_BY_VECTOR else s_rstd_end)
                            else:
                                shift(t)
                    else:
                        deviations(0, 2, s_rstd)
                        deviations(2, 2, s_rstd)
                        for t in range(TT):
                            shift(t)
                    if first and kind == NR:
                        split_items()

                return body

            over_batches(eng, step)


def kernel(x, itok_B_0_2, L0_cond_w1_nr, L0_cond_b1_nr, L0_cond_w2_nr, L0_cond_b2_nr, L0_cond_w1_tsr, L0_cond_b1_tsr,
           L0_cond_w2_tsr, L0_cond_b2_tsr, L0_cond_w1_sr, L0_cond_b1_sr, L0_cond_w2_sr, L0_cond_b2_sr, L0_cond_w3_sr,
           L0_cond_b3_sr, L0_cond_gamma, L0_cond_beta):
    import numpy as np
    import concourse.bacc as bacc
    from concourse.bass_utils import run_bass_kernel_spmd

    x = np.ascontiguousarray(x)

    def by_column(w):
        h, n = w.shape
        return np.asarray(w).reshape(P, HC, n // H, H).transpose(1, 2, 0, 3).reshape(-1, P, H)

    def by_chunk(w):
        return np.asarray(w).reshape(-1, P, H)

    chunks = np.concatenate([
        by_column(L0_cond_w1_nr), by_chunk(L0_cond_w2_nr), by_column(L0_cond_w1_sr), by_chunk(L0_cond_w2_sr),
        by_chunk(L0_cond_w3_sr), by_column(L0_cond_w1_tsr), by_chunk(L0_cond_w2_tsr)])
    arrays = {
        "x": x,
        "x_t": np.ascontiguousarray(
            x.reshape(NBATCH, P, TT, P, HC).transpose(0, 4, 3, 2, 1).reshape(NBATCH, 2, 2, P, T).transpose(0, 1, 3, 2, 4)
        ).reshape(NBATCH, 2, P, 2 * T),
        "cond": np.ascontiguousarray(itok_B_0_2),
        "weights": np.ascontiguousarray(chunks.reshape(N_WCHUNK // 2, 2, P, H).transpose(0, 2, 1, 3)).reshape(-1, P, 2 * H),
        "bias_cols": np.ascontiguousarray(np.concatenate([
            np.asarray(L0_cond_b1_nr), np.asarray(L0_cond_b1_tsr), np.asarray(L0_cond_b1_sr), np.asarray(L0_cond_b2_sr)]).reshape(N_BCOL, P).T),
        "rows": np.stack([np.asarray(a) for a in (L0_cond_b2_nr, L0_cond_b2_tsr, L0_cond_b3_sr, L0_cond_gamma, L0_cond_beta)]),
    }
    nc = bacc.Bacc("TRN2", target_bir_lowering=False, num_devices=1)
    args = [nc.dram_tensor(n, a.shape, mybir.dt.from_np(a.dtype), kind="ExternalInput").ap() for n, a in arrays.items()]
    out = nc.dram_tensor("out", x.shape, mybir.dt.float32, kind="ExternalOutput").ap()
    conditional_mlp(nc, *args, out)
    result = run_bass_kernel_spmd(nc, [arrays], core_ids=[0])
    return result.results[0]["out"]
```
